# Optimizing a Trainium2 kernel written in Bass

```python
import numpy as np
import jax
import jax.numpy as jnp

def _softmax(x, axis=-1):
    return jax.nn.softmax(x, axis=axis)

def _gelu(x):
    return jax.nn.gelu(x, approximate=True)

def _silu(x):
    return jax.nn.silu(x)

def _sigmoid(x):
    return jax.nn.sigmoid(x)

def _layernorm(x, axis=-1, eps=1e-05):
    m = jnp.mean(x, axis=axis, keepdims=True)
    v = jnp.var(x, axis=axis, keepdims=True)
    return (x - m) / jnp.sqrt(v + eps)

def _scatter_add(tgt, idx, src, axis=0):
    return tgt.at[idx].add(src)

def _segment_sum(src, seg, n):
    return jax.ops.segment_sum(src, seg, n)
kernel_name = 'mk_dlrm_tower_d1_rec_r8_0808de'

def setup_inputs(seed: int=0):
    np.random.seed(seed)
    _w = jnp.asarray

    def _rec_inputs():
        import jax
        import jax.numpy as jnp
        _tk = jax.random.key(seed)
        dense_ctx = jax.random.normal(jax.random.fold_in(_tk, 190), (1024, 16), jnp.float32)
        ids = jnp.stack([jax.random.randint(jax.random.fold_in(_tk, 200 + f), (1024,), 0, v, jnp.int32) for f, v in enumerate([1000, 1250, 1250, 125000, 12500, 1000, 125000, 1250, 125000, 1000, 12500, 12500, 125000, 1000, 125000, 1250, 12500, 1000, 1250, 1000, 1250, 1000, 125000, 125000, 1250, 12500, 1250, 1000, 1250, 1000, 1000, 125000, 1000, 125000, 1250, 125000, 12500, 125000, 1000])], axis=1)
        tbl_0 = 0.05 * jax.random.normal(jax.random.fold_in(_tk, 500 + 0), (1000, 16), jnp.float32)
        tbl_1 = 0.05 * jax.random.normal(jax.random.fold_in(_tk, 500 + 1), (1250, 16), jnp.float32)
        tbl_2 = 0.05 * jax.random.normal(jax.random.fold_in(_tk, 500 + 2), (1250, 16), jnp.float32)
        tbl_3 = 0.05 * jax.random.normal(jax.random.fold_in(_tk, 500 + 3), (125000, 16), jnp.float32)
        tbl_4 = 0.05 * jax.random.normal(jax.random.fold_in(_tk, 500 + 4), (12500, 16), jnp.float32)
        tbl_5 = 0.05 * jax.random.normal(jax.random.fold_in(_tk, 500 + 5), (1000, 16), jnp.float32)
        tbl_6 = 0.05 * jax.random.normal(jax.random.fold_in(_tk, 500 + 6), (125000, 16), jnp.float32)
        tbl_7 = 0.05 * jax.random.normal(jax.random.fold_in(_tk, 500 + 7), (1250, 16), jnp.float32)
        tbl_8 = 0.05 * jax.random.normal(jax.random.fold_in(_tk, 500 + 8), (125000, 16), jnp.float32)
        tbl_9 = 0.05 * jax.random.normal(jax.random.fold_in(_tk, 500 + 9), (1000, 16), jnp.float32)
        tbl_10 = 0.05 * jax.random.normal(jax.random.fold_in(_tk, 500 + 10), (12500, 16), jnp.float32)
        tbl_11 = 0.05 * jax.random.normal(jax.random.fold_in(_tk, 500 + 11), (12500, 16), jnp.float32)
        tbl_12 = 0.05 * jax.random.normal(jax.random.fold_in(_tk, 500 + 12), (125000, 16), jnp.float32)
        tbl_13 = 0.05 * jax.random.normal(jax.random.fold_in(_tk, 500 + 13), (1000, 16), jnp.float32)
        tbl_14 = 0.05 * jax.random.normal(jax.random.fold_in(_tk, 500 + 14), (125000, 16), jnp.float32)
        tbl_15 = 0.05 * jax.random.normal(jax.random.fold_in(_tk, 500 + 15), (1250, 16), jnp.float32)
        tbl_16 = 0.05 * jax.random.normal(jax.random.fold_in(_tk, 500 + 16), (12500, 16), jnp.float32)
        tbl_17 = 0.05 * jax.random.normal(jax.random.fold_in(_tk, 500 + 17), (1000, 16), jnp.float32)
        tbl_18 = 0.05 * jax.random.normal(jax.random.fold_in(_tk, 500 + 18), (1250, 16), jnp.float32)
        tbl_19 = 0.05 * jax.random.normal(jax.random.fold_in(_tk, 500 + 19), (1000, 16), jnp.float32)
        tbl_20 = 0.05 * jax.random.normal(jax.random.fold_in(_tk, 500 + 20), (1250, 16), jnp.float32)
        tbl_21 = 0.05 * jax.random.normal(jax.random.fold_in(_tk, 500 + 21), (1000, 16), jnp.float32)
        tbl_22 = 0.05 * jax.random.normal(jax.random.fold_in(_tk, 500 + 22), (125000, 16), jnp.float32)
        tbl_23 = 0.05 * jax.random.normal(jax.random.fold_in(_tk, 500 + 23), (125000, 16), jnp.float32)
        tbl_24 = 0.05 * jax.random.normal(jax.random.fold_in(_tk, 500 + 24), (1250, 16), jnp.float32)
        tbl_25 = 0.05 * jax.random.normal(jax.random.fold_in(_tk, 500 + 25), (12500, 16), jnp.float32)
        tbl_26 = 0.05 * jax.random.normal(jax.random.fold_in(_tk, 500 + 26), (1250, 16), jnp.float32)
        tbl_27 = 0.05 * jax.random.normal(jax.random.fold_in(_tk, 500 + 27), (1000, 16), jnp.float32)
        tbl_28 = 0.05 * jax.random.normal(jax.random.fold_in(_tk, 500 + 28), (1250, 16), jnp.float32)
        tbl_29 = 0.05 * jax.random.normal(jax.random.fold_in(_tk, 500 + 29), (1000, 16), jnp.float32)
        tbl_30 = 0.05 * jax.random.normal(jax.random.fold_in(_tk, 500 + 30), (1000, 16), jnp.float32)
        tbl_31 = 0.05 * jax.random.normal(jax.random.fold_in(_tk, 500 + 31), (125000, 16), jnp.float32)
        tbl_32 = 0.05 * jax.random.normal(jax.random.fold_in(_tk, 500 + 32), (1000, 16), jnp.float32)
        tbl_33 = 0.05 * jax.random.normal(jax.random.fold_in(_tk, 500 + 33), (125000, 16), jnp.float32)
        tbl_34 = 0.05 * jax.random.normal(jax.random.fold_in(_tk, 500 + 34), (1250, 16), jnp.float32)
        tbl_35 = 0.05 * jax.random.normal(jax.random.fold_in(_tk, 500 + 35), (125000, 16), jnp.float32)
        tbl_36 = 0.05 * jax.random.normal(jax.random.fold_in(_tk, 500 + 36), (12500, 16), jnp.float32)
        tbl_37 = 0.05 * jax.random.normal(jax.random.fold_in(_tk, 500 + 37), (125000, 16), jnp.float32)
        tbl_38 = 0.05 * jax.random.normal(jax.random.fold_in(_tk, 500 + 38), (1000, 16), jnp.float32)
        _rk = jax.random.fold_in(_tk, 7)
        W_top1 = 0.0606339 * jax.random.normal(jax.random.fold_in(_tk, 801), (272, 512), jnp.float32)
        W_top2 = 0.0441942 * jax.random.normal(jax.random.fold_in(_tk, 802), (512, 256), jnp.float32)
        W_top3 = 0.0625 * jax.random.normal(jax.random.fold_in(_tk, 803), (256, 1), jnp.float32)
        b_top1 = jnp.zeros((512,), jnp.float32)
        b_top2 = jnp.zeros((256,), jnp.float32)
        return (dense_ctx, ids, tbl_0, tbl_1, tbl_2, tbl_3, tbl_4, tbl_5, tbl_6, tbl_7, tbl_8, tbl_9, tbl_10, tbl_11, tbl_12, tbl_13, tbl_14, tbl_15, tbl_16, tbl_17, tbl_18, tbl_19, tbl_20, tbl_21, tbl_22, tbl_23, tbl_24, tbl_25, tbl_26, tbl_27, tbl_28, tbl_29, tbl_30, tbl_31, tbl_32, tbl_33, tbl_34, tbl_35, tbl_36, tbl_37, tbl_38, W_top1, b_top1, W_top2, b_top2, W_top3)
    dense_ctx, ids, tbl_0, tbl_1, tbl_2, tbl_3, tbl_4, tbl_5, tbl_6, tbl_7, tbl_8, tbl_9, tbl_10, tbl_11, tbl_12, tbl_13, tbl_14, tbl_15, tbl_16, tbl_17, tbl_18, tbl_19, tbl_20, tbl_21, tbl_22, tbl_23, tbl_24, tbl_25, tbl_26, tbl_27, tbl_28, tbl_29, tbl_30, tbl_31, tbl_32, tbl_33, tbl_34, tbl_35, tbl_36, tbl_37, tbl_38, W_top1, b_top1, W_top2, b_top2, W_top3 = _rec_inputs()

    def _L0_rec_setup():
        import jax, jax.numpy as jnp
        import numpy as np
        B, F0, D = (256, 39, 16)
        LAYER_SIZES = [128, 128, 128]
        key = jax.random.key(seed)
        ks = jax.random.split(key, 1 + 2 * len(LAYER_SIZES))
        inputs = jax.random.normal(ks[0], (B, F0, D), dtype=jnp.float32)
        out = {'inputs': inputs}
        field_nums = [F0]
        for i, size in enumerate(LAYER_SIZES):
            fk = field_nums[-1]
            fan_in = F0 * fk
            scale = np.sqrt(2.0 / (fan_in + size)).astype(np.float32)
            out[f'w{i}'] = jax.random.normal(ks[1 + 2 * i], (F0, fk, size), dtype=jnp.float32) * scale
            out[f'b{i}'] = jnp.zeros((size,), dtype=jnp.float32)
            field_nums.append(size // 2)
        return out
    _L0_rec_all = _L0_rec_setup()
    _L0_rec_in = {k: v for k, v in _L0_rec_all.items() if k in ('w0', 'w1', 'w2', 'b0', 'b1', 'b2')}
    del _L0_rec_all
    return {'dense_ctx': dense_ctx, 'ids': ids, 'tbl_0': tbl_0, 'tbl_1': tbl_1, 'tbl_2': tbl_2, 'tbl_3': tbl_3, 'tbl_4': tbl_4, 'tbl_5': tbl_5, 'tbl_6': tbl_6, 'tbl_7': tbl_7, 'tbl_8': tbl_8, 'tbl_9': tbl_9, 'tbl_10': tbl_10, 'tbl_11': tbl_11, 'tbl_12': tbl_12, 'tbl_13': tbl_13, 'tbl_14': tbl_14, 'tbl_15': tbl_15, 'tbl_16': tbl_16, 'tbl_17': tbl_17, 'tbl_18': tbl_18, 'tbl_19': tbl_19, 'tbl_20': tbl_20, 'tbl_21': tbl_21, 'tbl_22': tbl_22, 'tbl_23': tbl_23, 'tbl_24': tbl_24, 'tbl_25': tbl_25, 'tbl_26': tbl_26, 'tbl_27': tbl_27, 'tbl_28': tbl_28, 'tbl_29': tbl_29, 'tbl_30': tbl_30, 'tbl_31': tbl_31, 'tbl_32': tbl_32, 'tbl_33': tbl_33, 'tbl_34': tbl_34, 'tbl_35': tbl_35, 'tbl_36': tbl_36, 'tbl_37': tbl_37, 'tbl_38': tbl_38, 'W_top1': W_top1, 'b_top1': b_top1, 'W_top2': W_top2, 'b_top2': b_top2, 'W_top3': W_top3, 'L0_rec_w0': _L0_rec_in['w0'], 'L0_rec_w1': _L0_rec_in['w1'], 'L0_rec_w2': _L0_rec_in['w2'], 'L0_rec_b0': _L0_rec_in['b0'], 'L0_rec_b1': _L0_rec_in['b1'], 'L0_rec_b2': _L0_rec_in['b2']}

def reference(dense_ctx, ids, tbl_0, tbl_1, tbl_2, tbl_3, tbl_4, tbl_5, tbl_6, tbl_7, tbl_8, tbl_9, tbl_10, tbl_11, tbl_12, tbl_13, tbl_14, tbl_15, tbl_16, tbl_17, tbl_18, tbl_19, tbl_20, tbl_21, tbl_22, tbl_23, tbl_24, tbl_25, tbl_26, tbl_27, tbl_28, tbl_29, tbl_30, tbl_31, tbl_32, tbl_33, tbl_34, tbl_35, tbl_36, tbl_37, tbl_38, W_top1, b_top1, W_top2, b_top2, W_top3, L0_rec_w0, L0_rec_w1, L0_rec_w2, L0_rec_b0, L0_rec_b1, L0_rec_b2):
    import jax
    import jax.numpy as jnp

    def _L0_rec_ref(inputs, w0, w1, w2, b0, b1, b2):
        import jax, jax.numpy as jnp
        import numpy as np
        B, F0, D = (256, 39, 16)
        LAYER_SIZES = [128, 128, 128]
        x0 = inputs
        xk = inputs
        params = [(w0, b0), (w1, b1), (w2, b2)]
        n_layers = len(params)
        direct = []
        for idx, (W, b) in enumerate(params):
            z = jnp.einsum('bhd,bkd,hks->bsd', x0, xk, W) + b[None, :, None]
            z = jax.nn.relu(z)
            if idx != n_layers - 1:
                half = z.shape[1] // 2
                xk = z[:, :half, :]
                direct.append(z[:, half:, :])
            else:
                direct.append(z)
        logit = jnp.sum(jnp.concatenate(direct, axis=1), axis=-1)
        return logit
    e = jnp.stack([tbl_0[ids[:, 0]], tbl_1[ids[:, 1]], tbl_2[ids[:, 2]], tbl_3[ids[:, 3]], tbl_4[ids[:, 4]], tbl_5[ids[:, 5]], tbl_6[ids[:, 6]], tbl_7[ids[:, 7]], tbl_8[ids[:, 8]], tbl_9[ids[:, 9]], tbl_10[ids[:, 10]], tbl_11[ids[:, 11]], tbl_12[ids[:, 12]], tbl_13[ids[:, 13]], tbl_14[ids[:, 14]], tbl_15[ids[:, 15]], tbl_16[ids[:, 16]], tbl_17[ids[:, 17]], tbl_18[ids[:, 18]], tbl_19[ids[:, 19]], tbl_20[ids[:, 20]], tbl_21[ids[:, 21]], tbl_22[ids[:, 22]], tbl_23[ids[:, 23]], tbl_24[ids[:, 24]], tbl_25[ids[:, 25]], tbl_26[ids[:, 26]], tbl_27[ids[:, 27]], tbl_28[ids[:, 28]], tbl_29[ids[:, 29]], tbl_30[ids[:, 30]], tbl_31[ids[:, 31]], tbl_32[ids[:, 32]], tbl_33[ids[:, 33]], tbl_34[ids[:, 34]], tbl_35[ids[:, 35]], tbl_36[ids[:, 36]], tbl_37[ids[:, 37]], tbl_38[ids[:, 38]]], axis=1)
    z = _L0_rec_ref(e, L0_rec_w0, L0_rec_w1, L0_rec_w2, L0_rec_b0, L0_rec_b1, L0_rec_b2)
    z = z.reshape(z.shape[0], -1)
    h = jnp.concatenate([z, dense_ctx], axis=1)
    h = jnp.maximum(h @ W_top1 + b_top1, 0.0)
    h = jnp.maximum(h @ W_top2 + b_top2, 0.0)
    y = h @ W_top3
    return y

_drawn_inputs = setup_inputs


def setup_inputs(seed=0):
    import zlib

    import numpy as np

    out = dict(_drawn_inputs(seed))
    spreads = {'b_top1': (0.0, 2.0),
     'b_top2': (0.0, 2.0),
     'L0_rec_b0': (0.0, 0.339),
     'L0_rec_b1': (0.0, 0.532),
     'L0_rec_b2': (0.0, 0.8)}
    factors = {'tbl_0': 8.0,
     'tbl_1': 8.0,
     'tbl_2': 8.0,
     'tbl_3': 8.0,
     'tbl_4': 8.0,
     'tbl_5': 8.0,
     'tbl_6': 8.0,
     'tbl_7': 8.0,
     'tbl_8': 8.0,
     'tbl_9': 8.0,
     'tbl_10': 8.0,
     'tbl_11': 8.0,
     'tbl_12': 8.0,
     'tbl_13': 8.0,
     'tbl_14': 8.0,
     'tbl_15': 8.0,
     'tbl_16': 8.0,
     'tbl_17': 8.0,
     'tbl_18': 8.0,
     'tbl_19': 8.0,
     'tbl_20': 8.0,
     'tbl_21': 8.0,
     'tbl_22': 8.0,
     'tbl_23': 8.0,
     'tbl_24': 8.0,
     'tbl_25': 8.0,
     'tbl_26': 8.0,
     'tbl_27': 8.0,
     'tbl_28': 8.0,
     'tbl_29': 8.0,
     'tbl_30': 8.0,
     'tbl_31': 8.0,
     'tbl_32': 8.0,
     'tbl_33': 8.0,
     'tbl_34': 8.0,
     'tbl_35': 8.0,
     'tbl_36': 8.0,
     'tbl_37': 8.0,
     'tbl_38': 8.0,
     'L0_rec_w0': 8.0,
     'L0_rec_w1': 6.195,
     'L0_rec_w2': 4.8,
     'dense_ctx': 8.0}
    for name, (base, spread) in spreads.items():
        noise = np.random.default_rng([zlib.crc32(name.encode()), seed]).standard_normal(out[name].shape)
        drawn = base * np.exp(spread * noise) if base else spread * noise
        out[name] = jnp.asarray(drawn.astype(out[name].dtype))
    for name, factor in factors.items():
        out[name] = (out[name] * factor).astype(out[name].dtype)
    return out
```

```python
from contextlib import ExitStack

import concourse.bass as bass
from concourse import mybir

F32 = mybir.dt.float32
I32 = mybir.dt.int32
ALU = mybir.AluOpType
ACT = mybir.ActivationFunctionType
AX_X = mybir.AxisListType.X

P = 128
FIELDS = 39
DIM = 16
SHIFTS = FIELDS // 2 + 1
SPC = P // FIELDS
ROWS0 = SPC * FIELDS
CHUNKS0 = -(-SHIFTS // SPC)
XROWS = FIELDS + CHUNKS0 * SPC - 1
UNITS = 128
HALF = UNITS // 2
CHUNKS = (FIELDS + 1) // 2
N = 512
DPT = N // P
TPB = DIM // DPT
PAIRS = CHUNKS // 2
PAIRS0 = -(-CHUNKS0 // 2)
PER_STEP = 2 * PAIRS + PAIRS0
SLOTS = 6
LOADS = 5
CPL = CHUNKS // LOADS
AHEAD = 2


class Tile:

    def __init__(self, first, turn=None):
        self.first, self.turn = first, turn

    def plus(self, n):
        return Tile(self.first + n, self.turn)

    def count(self, each, offset=0):
        fixed = each * self.first + offset
        return fixed if self.turn is None else self.turn * (each * TPB) + fixed

    def blocks(self, each=1, offset=0):
        fixed = each * (self.first // TPB) + offset
        return fixed if self.turn is None else self.turn * each + fixed

    def visits(self, ring, each=1, offset=0):
        fixed = each * (self.first // ring) + offset
        return fixed if self.turn is None else self.turn * (each * TPB // ring) + fixed


def wait(eng, semaphore, value):
    if not isinstance(value, int) or value > 0:
        eng.wait_ge(semaphore, value)


def build_kernel(nc, dense_ctx, ids, tables, W_top1, b_top1, W_top2, b_top2, W_top3,
                 w0, w1, w2, b0, b1, b2, y):
    B = ids.shape[0]
    BLOCKS = B // P
    TILES = BLOCKS * TPB
    CTX = dense_ctx.shape[1]
    T1 = W_top1.shape[1]
    T2 = W_top2.shape[1]
    M1, M2 = T1 // P, T2 // P
    LOOP0 = AHEAD
    TURNS = (TILES - 2 * AHEAD) // TPB
    WEIGHT_LOADS = 14

    x_rows = nc.dram_tensor("x_rows", (TILES, XROWS, N), F32, kind="Internal").ap()
    w0_k = nc.dram_tensor("w0_k", (FIELDS, XROWS, UNITS), F32, kind="Internal").ap()
    w0_h = nc.dram_tensor("w0_h", (XROWS, FIELDS, UNITS), F32, kind="Internal").ap()

    with ExitStack() as ctx:
        def sb(name, shape, dt=F32):
            return ctx.enter_context(nc.sbuf_tensor(name, shape, dt))

        def bank(name):
            return ctx.enter_context(nc.psum_tensor(name, [P, N], F32))

        def sem(name):
            return ctx.enter_context(nc.semaphore(name))

        ident = sb("ident", [P, P])
        w0s = sb("w0s", [P, CHUNKS0, UNITS])
        w1s = sb("w1s", [P, CHUNKS, UNITS])
        w2s = sb("w2s", [P, CHUNKS, UNITS])
        bias = sb("bias", [P, 3])
        bias_t1 = sb("bias_t1", [P, M1])
        bias_t2 = sb("bias_t2", [P, M2])
        wt1 = sb("wt1", [P, 2, T1])
        wt1c = sb("wt1c", [CTX, T1])
        wt2 = sb("wt2", [P, M1, T2])
        wt3 = sb("wt3", [P, M2])
        ctx_rows = sb("ctx_rows", [P, BLOCKS, CTX])

        idx_all = sb("idx_all", [P, BLOCKS, FIELDS], I32)
        idx = sb("idx", [P, FIELDS], I32)
        gathered = sb("gathered", [P, FIELDS, DIM])
        emb = sb("emb", [P, SPC, FIELDS * DIM])
        xt = sb("xt", [FIELDS, 2, N])
        x_shift = sb("x_shift", [ROWS0, CHUNKS0, N])
        x_rep = sb("x_rep", [P, 2, CHUNKS, N])
        prod = sb("prod", [P, SLOTS, 2, N])
        w0a, w0b = (prod[:, slot].rearrange("p a n -> p (a n)")[:, 0:CHUNKS0 * UNITS]
                    .rearrange("p (c s) -> p c s", s=UNITS) for slot in range(2))
        flat = x_rep[:].rearrange("p a c n -> p (a c n)")
        h1 = flat[:, 0:M1 * B].rearrange("p (m n) -> p m n", m=M1)
        h2 = flat[:, M1 * B:(M1 + M2) * B].rearrange("p (m n) -> p m n", m=M2)
        ctx_t = flat[0:CTX, (M1 + M2) * B:(M1 + M2 + 1) * B]
        y_row = flat[0:1, (M1 + M2 + 1) * B:(M1 + M2 + 2) * B]
        direct01 = sb("direct01", [P, TPB, N])
        direct2 = sb("direct2", [P, TPB, N])
        sum01 = sb("sum01", [P, B])
        sum2 = sb("sum2", [P, B])

        z = [bank("z_even"), bank("z_odd")]
        x0_bank = [bank("x0_even"), bank("x0_odd")]
        x1_bank = bank("x1_bank")
        x2_bank = bank("x2_bank")
        mlp = [bank("mlp_even"), bank("mlp_odd")]

        s_w0_ext = sem("w0_extended")
        s_w0_load = sem("w0_loaded")
        s_w0_zero = sem("w0_zeroed")
        s_w0 = sem("w0_ready")
        s_w12_zero = sem("w12_zeroed")
        s_w = sem("weights_loaded")
        s_ident0 = sem("ident_zeroed")
        s_ident = sem("ident_ready")
        s_ids = sem("ids_loaded")
        s_idx = sem("idx_ready")
        s_gather = sem("gather_landed")
        s_emb = sem("emb_ready")
        s_x0 = sem("x0_transposed")
        s_xt = sem("xt_ready")
        s_stored = sem("x_rows_stored")
        s_shift = sem("x_shift_loaded")
        s_rep = [[sem(f"x_rep_loaded_{p}_{g}") for g in range(LOADS)] for p in range(2)]
        s_prod = sem("prod_ready")
        s_used = sem("prod_used")
        s_x1 = sem("x1_ready")
        s_x2 = sem("x2_ready")
        s_d01 = sem("direct01_ready")
        s_d2 = sem("direct2_ready")
        s_sum01 = sem("sum01_ready")
        s_sum2 = sem("sum2_ready")
        s_ctx_t = sem("ctx_transposed")
        s_ctx = sem("ctx_ready")
        s_mm = sem("mlp_bank_full")
        s_act = sem("mlp_bank_read")
        s_out = sem("y_stored")

        def products(t, layer):
            if t.turn is None and t.first < 0:
                return 0
            last = t.turn is None and t.first == TILES - 1
            skipped = PAIRS0 if last and layer == 2 else 0
            return t.count(PER_STEP, PAIRS0 + {1: 0, 0: PAIRS, 2: PAIRS + PAIRS0}[layer] - skipped)

        def first_slot(t, layer):
            return products(Tile(t.first), layer) % SLOTS

        def stage(t, layer):
            if t.turn is None and t.first < 0:
                return 0
            last = t.turn is None and t.first == TILES - 1
            return t.count(3, {1: 1, 0: 2, 2: 3}[layer] - (1 if last and layer == 2 else 0))

        def z_of(t, layer):
            return z[stage(Tile(t.first), layer) % 2]

        def steps(eng, body):
            for t in range(-AHEAD, LOOP0):
                body(Tile(t))
            with eng.Fori(0, TURNS) as turn:
                for k in range(TPB):
                    body(Tile(LOOP0 + k, turn))
            for t in range(LOOP0 + TURNS * TPB, TILES):
                body(Tile(t))

        def has_layers12(t):
            return t.turn is not None or t.first >= 0

        def has_layer0(t):
            return t.turn is not None or -1 <= t.first < TILES - 1

        def has_transposes(t):
            return t.turn is not None or t.first < TILES - AHEAD

        block = ctx.enter_context(nc.Block())

        @block.sync
        def _(sp):
            sp.dma_start(idx_all[:], ids.rearrange("(b p) f -> p b f", p=P)).then_inc(s_ids, 16)
            sp.dma_start(w0_k[:, 0:FIELDS, :], w0).then_inc(s_w0_ext, 16)
            sp.dma_start(w0_k[:, FIELDS:, :], w0[:, 0:XROWS - FIELDS, :]).then_inc(s_w0_ext, 16)
            sp.dma_start(w0_h[0:FIELDS, :, :], w0).then_inc(s_w0_ext, 16)
            sp.dma_start(w0_h[FIELDS:, :, :], w0[0:XROWS - FIELDS, :, :]).then_inc(s_w0_ext, 16)
            sp.wait_ge(s_w0_ext, 64)
            sp.wait_ge(s_w0_zero, 2)
            kf = w0_k.rearrange("h k s -> (h k) s")
            hf = w0_h.rearrange("h k s -> (h k) s")
            for r in range(SPC):
                n = CHUNKS0 - (SPC * (CHUNKS0 - 1) + r >= SHIFTS)
                rows = slice(FIELDS * r, FIELDS * (r + 1))
                sp.dma_start(w0a[rows, 0:n, :], bass.AP(
                    tensor=kf.tensor, offset=r * UNITS,
                    ap=[[(XROWS + 1) * UNITS, FIELDS], [SPC * UNITS, n], [1, UNITS]])).then_inc(s_w0_load, 16)
                c0 = 1 if r == 0 else 0
                sp.dma_start(w0b[rows, c0:n, :], bass.AP(
                    tensor=hf.tensor, offset=(SPC * c0 + r) * FIELDS * UNITS,
                    ap=[[(FIELDS + 1) * UNITS, FIELDS], [SPC * FIELDS * UNITS, n - c0],
                        [1, UNITS]])).then_inc(s_w0_load, 16)
            whole = (CHUNKS - 1) * P
            sp.wait_ge(s_w12_zero, 2)
            for w, ws in ((w1, w1s), (w2, w2s)):
                rows = w.rearrange("h k s -> (h k) s")
                sp.dma_start(ws[:, 0:CHUNKS - 1, :],
                             rows[0:whole].rearrange("(c p) s -> p c s", p=P)).then_inc(s_w, 16)
                sp.dma_start(ws[0:HALF, CHUNKS - 1, :], rows[whole:]).then_inc(s_w, 16)
            for n, b in enumerate((b0, b1, b2)):
                sp.dma_start(bias[:, n:n + 1], b.rearrange("(s a) -> s a", a=1)).then_inc(s_w, 16)
            sp.dma_start(bias_t1[:], b_top1.rearrange("(m p) -> p m", p=P), allow_slow_non_contiguous=True).then_inc(s_w, 16)
            sp.dma_start(bias_t2[:], b_top2.rearrange("(m p) -> p m", p=P), allow_slow_non_contiguous=True).then_inc(s_w, 16)
            sp.dma_start(wt1[:], W_top1[0:2 * P].rearrange("(c p) m -> p c m", p=P)).then_inc(s_w, 16)
            sp.dma_start(wt1c[:], W_top1[2 * P:]).then_inc(s_w, 16)
            sp.dma_start(wt2[:], W_top2.rearrange("(c p) m -> p c m", p=P)).then_inc(s_w, 16)
            sp.dma_start(wt3[:], W_top3.rearrange("(c p) a -> p (c a)", p=P), allow_slow_non_contiguous=True).then_inc(s_w, 16)
            sp.dma_start(ctx_rows[:], dense_ctx.rearrange("(b p) c -> p b c", p=P)).then_inc(s_w, 16)

            def source(row, first, pattern):
                return bass.AP(tensor=row.tensor, offset=row.offset + first * N, ap=pattern)

            def body(t):
                if has_layer0(t):
                    nxt = t.plus(1)
                    par = nxt.first % 2
                    row = x_rows[nxt.count(1)] if nxt.turn is None else x_rows[bass.ds(nxt.count(1), 1)]
                    for g in range(LOADS):
                        if t.turn is not None or t.first >= 1:
                            wait(sp, s_prod, products(t.plus(-1), 2) + (g + 1) * (CPL // 2))
                        for half in range(2):
                            src = source(row, 2 * CPL * g + half, [[0, HALF], [2 * N, CPL], [1, N]])
                            sp.dma_start(x_rep[HALF * half:HALF * (half + 1), par, CPL * g:CPL * (g + 1), :],
                                         src).then_inc(s_rep[par][g], 16)
                if has_transposes(t):
                    nxt = t.plus(AHEAD)
                    row = x_rows[nxt.count(1)] if nxt.turn is None else x_rows[bass.ds(nxt.count(1), 1)]
                    wait(sp, s_xt, nxt.count(1, 1))
                    now = xt[:, nxt.first % 2, :]
                    sp.dma_start(source(row, 0, [[N, FIELDS], [1, N]]), now).then_inc(s_stored, 16)
                    if has_layer0(t):
                        wait(sp, s_prod, products(t, 0) + PAIRS0)
                    sp.dma_start(source(row, FIELDS, [[N, XROWS - FIELDS], [1, N]]),
                                 now[0:XROWS - FIELDS, :]).then_inc(s_stored, 16)
                    wait(sp, s_stored, nxt.count(32, 32))
                    for r in range(SPC):
                        src = source(row, r, [[N, FIELDS], [SPC * N, CHUNKS0], [1, N]])
                        sp.dma_start(x_shift[FIELDS * r:FIELDS * (r + 1), :, :], src).then_inc(s_shift, 16)

            steps(sp, body)
            sp.wait_ge(s_w0_load, 16 * 2 * SPC)
            sp.wait_ge(s_out, 16)

        @block.gpsimd
        def _(pool):
            def gather(b):
                if not isinstance(b, int) or b >= 1:
                    pool.wait_ge(s_emb, b * 1)
                src = idx_all[:, b, :] if isinstance(b, int) else idx_all[:, bass.ds(b, 1), :]
                nc.gpsimd.tensor_copy(idx[:], src).then_inc(s_idx, 1)
                pool.wait_ge(s_idx, b + 1)
                if not isinstance(b, int):
                    pool.reg_add(landed, landed, 16 * FIELDS)
                for f in range(FIELDS):
                    nc.gpsimd.indirect_dma_start(
                        gathered[:, f, :], None, tables[f],
                        bass.IndirectOffsetOnAxis(ap=idx[:, f:f + 1], axis=0)).then_inc(s_gather, 16)
                pool.wait_ge(s_gather, 16 * FIELDS * (b + 1) if isinstance(b, int) else
                             pool.snap(landed, min_val=16 * FIELDS, max_val=16 * FIELDS * BLOCKS))

            landed = pool.alloc_register("landed")
            pool.reg_mov(landed, 2 * 16 * FIELDS)
            pool.wait_ge(s_ids, 16)
            gather(0)
            pool.wait_ge(s_ident0, 1)
            nc.gpsimd.affine_select(out=ident[:], in_=ident[:], compare_op=ALU.not_equal, fill=1.0, base=0,
                                    pattern=[[-1, P]], channel_multiplier=1).then_inc(s_ident, 1)
            gather(1)
            with pool.Fori(2, BLOCKS) as b:
                gather(b)

        @block.scalar
        def _(act):
            act.wait_ge(s_w, 16 * WEIGHT_LOADS)

            def relu(out, z_rows, b):
                return nc.scalar.activation(out, z_rows, ACT.Relu, bias=b)

            def body(t):
                if has_transposes(t):
                    nxt = t.plus(AHEAD)
                    if nxt.first % TPB == 0:
                        wait(act, s_gather, nxt.blocks(16 * FIELDS, 16 * FIELDS))
                        wait(act, s_x0, nxt.count(1))
                        nc.scalar.copy(emb[:], gathered[:].rearrange("p f d -> p (f d)").unsqueeze(1)
                                       .to_broadcast([P, SPC, FIELDS * DIM])).then_inc(s_emb, 1)
                    wait(act, s_x0, nxt.count(1, 1))
                    wait(act, s_stored, nxt.count(32, -32))
                    nc.scalar.copy(xt[:, nxt.first % 2, :],
                                   x0_bank[nxt.first % 2][0:FIELDS, :]).then_inc(s_xt, 1)
                if has_layers12(t):
                    zz = z_of(t, 1)
                    wait(act, s_used, products(t, 1) + PAIRS)
                    relu(x2_bank[0:HALF, :], zz[0:HALF, :], bias[0:HALF, 1:2]).then_inc(s_x2, 1)
                    relu(x2_bank[HALF:P, :], zz[0:HALF, :], bias[0:HALF, 1:2]).then_inc(s_x2, 1)
                    if t.first % TPB == 0:
                        wait(act, s_sum01, t.blocks())
                    relu(direct01[HALF:P, t.first % TPB, :], zz[HALF:P, :],
                         bias[HALF:P, 1:2]).then_inc(s_d01, 1)
                if has_layer0(t):
                    nxt = t.plus(1)
                    zz = z_of(t, 0)
                    wait(act, s_used, products(t, 0) + PAIRS0)
                    relu(x1_bank[0:HALF, :], zz[0:HALF, :], bias[0:HALF, 0:1]).then_inc(s_x1, 1)
                    relu(x1_bank[HALF:P, :], zz[0:HALF, :], bias[0:HALF, 0:1]).then_inc(s_x1, 1)
                    if nxt.first % TPB == 0:
                        wait(act, s_sum01, nxt.blocks())
                    relu(direct01[0:HALF, nxt.first % TPB, :], zz[HALF:P, :],
                         bias[HALF:P, 0:1]).then_inc(s_d01, 1)
                if has_layers12(t):
                    zz = z_of(t, 2)
                    wait(act, s_used, products(t, 2) + PAIRS)
                    if t.first % TPB == 0:
                        wait(act, s_sum2, t.blocks())
                    relu(direct2[:, t.first % TPB, :], zz[:], bias[:, 2:3]).then_inc(s_d2, 1)
            steps(act, body)

            act.wait_ge(s_ctx_t, 1)
            for half in range(B // N):
                nc.scalar.copy(ctx_t[:, half * N:(half + 1) * N], mlp[half][0:CTX, :]).then_inc(s_ctx, 1)
            n = 0
            for half in range(B // N):
                for m in range(M1):
                    act.wait_ge(s_mm, n + 1)
                    relu(h1[:, m, half * N:(half + 1) * N], mlp[n % 2][:], bias_t1[:, m:m + 1]).then_inc(s_act, 1)
                    n += 1
                for m in range(M2):
                    act.wait_ge(s_mm, n + 1)
                    relu(h2[:, m, half * N:(half + 1) * N], mlp[n % 2][:], bias_t2[:, m:m + 1]).then_inc(s_act, 1)
                    n += 1
                act.wait_ge(s_mm, n + 1)
                nc.scalar.copy(y_row[:, half * N:(half + 1) * N], mlp[n % 2][0:1, :]).then_inc(s_act, 1)
                n += 1
            act.wait_ge(s_act, n)
            act.dma_start(y.rearrange("b a -> a b"), y_row).then_inc(s_out, 16)
            act.wait_ge(s_out, 16)

        @block.vector
        def _(dve):
            for w in (w0a, w0b):
                nc.vector.memset(w, 0.0).then_inc(s_w0_zero, 1)
            for w in (w1s, w2s):
                nc.vector.memset(w[HALF:P, CHUNKS - 1, :], 0.0).then_inc(s_w12_zero, 1)
            nc.vector.memset(ident[:], 0.0).then_inc(s_ident0, 1)
            dve.wait_ge(s_w0_load, 16 * 2 * SPC)
            nc.vector.tensor_tensor(w0s[0:ROWS0], w0a[0:ROWS0], w0b[0:ROWS0], ALU.add).then_inc(s_w0, 1)
            dve.wait_ge(s_w0, 1)

            def product(t, layer, j, xk, x0, rows):
                slot = (first_slot(t, layer) + j) % SLOTS
                wait(dve, s_used, products(t, layer) + (j + 1 - SLOTS))
                width = x0.shape[1]
                nc.vector.tensor_tensor(prod[0:rows, slot, 0:width, :],
                                        xk[0:rows, :].unsqueeze(1).to_broadcast([rows, width, N]),
                                        x0, ALU.mult).then_inc(s_prod, 1)

            def layer12(t, layer, xk, pairs):
                par = t.first % 2
                for j in pairs:
                    if layer == 1 and (2 * j) % CPL == 0:
                        g = 2 * j // CPL
                        dve.wait_ge(s_rep[par][g], t.visits(2, 32, 32))
                    product(t, layer, j, xk, x_rep[:, par, 2 * j:2 * j + 2, :], P)

            def add_dims(out, direct, t, done):
                b = t.blocks()
                cols = out[:, b * P:(b + 1) * P] if t.turn is None else out[:, bass.ds(b * P, P)]
                nc.vector.tensor_reduce(cols, direct[:].rearrange("p t (d b) -> p b (t d)", d=DPT),
                                        AX_X, ALU.add).then_inc(done, 1)

            def body(t):
                if has_layers12(t):
                    dve.wait_ge(s_x1, t.count(2, 2))
                    layer12(t, 1, x1_bank, range(PAIRS))
                if has_layer0(t):
                    nxt = t.plus(1)
                    dve.wait_ge(s_xt, nxt.count(1, 1))
                    dve.wait_ge(s_shift, nxt.count(16 * SPC, 16 * SPC))
                    for j in range(PAIRS0):
                        c = slice(2 * j, min(2 * j + 2, CHUNKS0))
                        product(t, 0, j, x0_bank[nxt.first % 2], x_shift[:, c, :], ROWS0)
                if has_layers12(t):
                    dve.wait_ge(s_x2, t.count(2, 2))
                    layer12(t, 2, x2_bank, range(3))
                    if t.first % TPB == TPB - 1:
                        dve.wait_ge(s_d01, t.count(2, 2))
                        add_dims(sum01, direct01, t, s_sum01)
                    layer12(t, 2, x2_bank, range(3, PAIRS))
                    if t.first % TPB == TPB - 1:
                        dve.wait_ge(s_d2, t.count(1, 1))
                        add_dims(sum2, direct2, t, s_sum2)

            steps(dve, body)

        @block.tensor
        def _(pe):
            pe.wait_ge(s_ident, 1)
            pe.wait_ge(s_w0, 1)
            pe.wait_ge(s_w, 16 * WEIGHT_LOADS)

            def layer(t, which, weights, rows, j, chunks, last):
                zz = z_of(t, which)
                pe.wait_ge(s_prod, products(t, which) + (j + 1))
                slot = (first_slot(t, which) + j) % SLOTS
                for i, c in enumerate(chunks):
                    mm = nc.tensor.matmul(zz[:], weights[0:rows, c, :], prod[0:rows, slot, i, :],
                                          start=(c == 0), stop=(c == last))
                mm.then_inc(s_used, 1)

            def body(t):
                if has_layers12(t):
                    wait(pe, s_d01, t.count(2, 1))
                    for j in range(PAIRS // 2):
                        layer(t, 1, w1s, P, j, (2 * j, 2 * j + 1), CHUNKS - 1)
                if has_transposes(t):
                    nxt = t.plus(AHEAD)
                    if nxt.first % TPB == 0:
                        wait(pe, s_emb, nxt.blocks(1, 1))
                    wait(pe, s_prod, products(t.plus(-1), 0) + PAIRS0 if has_layers12(t) else 0)
                    out = x0_bank[nxt.first % 2]
                    for i in range(DPT):
                        d = nxt.first % TPB * DPT + i
                        rows = emb[:].rearrange("p r (f d) -> p (r f) d", d=DIM)[:, :, d]
                        mm = nc.tensor.transpose(out[0:ROWS0, i * P:(i + 1) * P], rows, ident[:])
                    mm.then_inc(s_x0, 1)
                if has_layers12(t):
                    for j in range(PAIRS // 2, PAIRS):
                        layer(t, 1, w1s, P, j, (2 * j, 2 * j + 1), CHUNKS - 1)
                if has_layer0(t):
                    if has_layers12(t):
                        wait(pe, s_d2, t.count(1))
                    for j in range(PAIRS0):
                        layer(t, 0, w0s, ROWS0, j, range(2 * j, min(2 * j + 2, CHUNKS0)), CHUNKS0 - 1)
                if has_layers12(t):
                    if has_layer0(t):
                        wait(pe, s_d01, t.count(2, 2))
                    else:
                        wait(pe, s_d2, t.count(1))
                    for j in range(PAIRS):
                        layer(t, 2, w2s, P, j, (2 * j, 2 * j + 1), CHUNKS - 1)

            steps(pe, body)

            for b in range(BLOCKS):
                mm = nc.tensor.transpose(mlp[b * P // N][0:CTX, b * P % N:b * P % N + P], ctx_rows[:, b, :], ident[:])
            mm.then_inc(s_ctx_t, 1)
            pe.wait_ge(s_ctx, 2)
            pe.wait_ge(s_sum01, BLOCKS)
            pe.wait_ge(s_sum2, BLOCKS)
            n = 0
            for half in range(B // N):
                cols = slice(half * N, (half + 1) * N)
                for m in range(M1):
                    pe.wait_ge(s_act, n - 1) if n >= 2 else None
                    units = slice(m * P, (m + 1) * P)
                    nc.tensor.matmul(mlp[n % 2][:], wt1[:, 0, units], sum01[:, cols], start=True, stop=False)
                    nc.tensor.matmul(mlp[n % 2][:], wt1[:, 1, units], sum2[:, cols], start=False, stop=False)
                    nc.tensor.matmul(mlp[n % 2][:], wt1c[:, units], ctx_t[:, cols], start=False,
                                     stop=True).then_inc(s_mm, 1)
                    n += 1
                h1_done = n
                for m in range(M2):
                    pe.wait_ge(s_act, h1_done)
                    for c in range(M1):
                        mm = nc.tensor.matmul(mlp[n % 2][:], wt2[:, c, m * P:(m + 1) * P], h1[:, c, cols],
                                              start=(c == 0), stop=(c == M1 - 1))
                    mm.then_inc(s_mm, 1)
                    n += 1
                pe.wait_ge(s_act, n)
                for c in range(M2):
                    mm = nc.tensor.matmul(mlp[n % 2][0:1, :], wt3[:, c:c + 1], h2[:, c, cols],
                                          start=(c == 0), stop=(c == M2 - 1))
                mm.then_inc(s_mm, 1)
                n += 1


def kernel(**inputs):
    import numpy as np
    import concourse.bacc as bacc
    from concourse.bass_utils import run_bass_kernel_spmd

    tables = [f"tbl_{f}" for f in range(FIELDS)]
    rest = ["W_top1", "b_top1", "W_top2", "b_top2", "W_top3",
            "L0_rec_w0", "L0_rec_w1", "L0_rec_w2", "L0_rec_b0", "L0_rec_b1", "L0_rec_b2"]
    nc = bacc.Bacc("TRN2", target_bir_lowering=False, num_devices=1)
    arrays, aps = {}, {}
    for name in ["dense_ctx", "ids"] + tables + rest:
        a = np.ascontiguousarray(inputs[name])
        arrays["in_" + name] = a
        aps[name] = nc.dram_tensor("in_" + name, a.shape, mybir.dt.from_np(a.dtype), kind="ExternalInput").ap()
    y = nc.dram_tensor("y", (inputs["ids"].shape[0], 1), F32, kind="ExternalOutput").ap()
    build_kernel(nc, aps["dense_ctx"], aps["ids"], [aps[t] for t in tables], *[aps[n] for n in rest], y)
    result = run_bass_kernel_spmd(nc, [arrays], core_ids=[0])
    return result.results[0]["y"]
```

```python
from contextlib import ExitStack

import concourse.bass as bass
from concourse import mybir

F32 = mybir.dt.float32
F32R = mybir.dt.float32r
I32 = mybir.dt.int32
ALU = mybir.AluOpType
ACT = mybir.ActivationFunctionType
AX_X = mybir.AxisListType.X

P = 128
FIELDS = 39
DIM = 16
SHIFTS = FIELDS // 2 + 1
SPC = P // FIELDS
ROWS0 = SPC * FIELDS
CHUNKS0 = -(-SHIFTS // SPC)
XROWS = FIELDS + CHUNKS0 * SPC - 1
UNITS = 128
HALF = UNITS // 2
CHUNKS = (FIELDS + 1) // 2
N = 512
DPT = N // P
TPB = DIM // DPT
PAIRS = CHUNKS // 2
PAIRS0 = -(-CHUNKS0 // 2)
KINDS = {1: "UVPPUPVPVP", 0: "UUUU", 2: "UUVUPUVPVP"}
ORDER = (1, 0, 2)
WHOLE_SLOTS = 6
SPLIT_SLOTS = 4
GATHERS_BETWEEN = 11
HEADS_IN_1 = 3
HEADS_IN_2 = 1
TRANSPOSES_AFTER = 2
ADD_2_AFTER = 4
ADD_01_AFTER = 1
DEFER = 2
LOADS = 5
CPL = CHUNKS // LOADS
TWICE = 2
TOGETHER = 2
AHEAD = 2


class Tile:

    def __init__(self, first, turn=None):
        self.first, self.turn = first, turn

    def plus(self, n):
        return Tile(self.first + n, self.turn)

    def count(self, each, offset=0):
        fixed = each * self.first + offset
        return fixed if self.turn is None else self.turn * (each * TPB) + fixed

    def blocks(self, each=1, offset=0):
        fixed = each * (self.first // TPB) + offset
        return fixed if self.turn is None else self.turn * each + fixed

    def visits(self, ring, each=1, offset=0):
        fixed = each * (self.first // ring) + offset
        return fixed if self.turn is None else self.turn * (each * TPB // ring) + fixed


def wait(eng, semaphore, value):
    if not isinstance(value, int) or value > 0:
        eng.wait_ge(semaphore, value)


def build_kernel(nc, dense_ctx, ids, tables, W_top1, b_top1, W_top2, b_top2, W_top3,
                 w0, w1, w2, b0, b1, b2, y):
    B = ids.shape[0]
    BLOCKS = B // P
    TILES = BLOCKS * TPB
    CTX = dense_ctx.shape[1]
    T1 = W_top1.shape[1]
    T2 = W_top2.shape[1]
    M1, M2 = T1 // P, T2 // P
    LOOP0 = AHEAD
    TURNS = (TILES - 2 * AHEAD) // TPB
    WEIGHT_LOADS = 11

    x_rows = nc.dram_tensor("x_rows", (TILES, XROWS, N), F32, kind="Internal").ap()
    w0_k = nc.dram_tensor("w0_k", (FIELDS, XROWS, UNITS), F32, kind="Internal").ap()
    w0_h = nc.dram_tensor("w0_h", (XROWS, FIELDS, UNITS), F32, kind="Internal").ap()

    with ExitStack() as ctx:
        def sb(name, shape, dt=F32):
            return ctx.enter_context(nc.sbuf_tensor(name, shape, dt))

        def bank(name):
            return ctx.enter_context(nc.psum_tensor(name, [P, N], F32))

        def sem(name):
            return ctx.enter_context(nc.semaphore(name))

        ident = sb("ident", [P, P])
        w0s = sb("w0s", [P, CHUNKS0, UNITS])
        split_chunks = [(layer, 2 * j + i) for layer in (1, 2) for j in range(PAIRS)
                        for i in range(2) if KINDS[layer][j] != "U"]
        whole_chunks = [(layer, 2 * j + i) for layer in (1, 2) for j in range(PAIRS)
                        for i in range(2) if KINDS[layer][j] == "U"]
        w_whole = sb("w_whole", [P, len(whole_chunks), UNITS])
        w_head = sb("w_head", [P, len(split_chunks), UNITS], F32R)
        w_rest = sb("w_rest", [P, len(split_chunks), UNITS], F32R)
        bias = sb("bias", [P, 3])
        bias_t1 = sb("bias_t1", [P, M1])
        bias_t2 = sb("bias_t2", [P, M2])
        wt3 = sb("wt3", [P, M2])
        ctx_rows = sb("ctx_rows", [P, BLOCKS, CTX])
        ctx_t = sb("ctx_t", [CTX, B])

        idx_all = sb("idx_all", [P, BLOCKS, FIELDS], I32)
        idx = sb("idx", [P, FIELDS], I32)
        gathered = sb("gathered", [P, FIELDS, DIM])
        emb = sb("emb", [P, SPC, FIELDS * DIM])
        xt = sb("xt", [FIELDS, 2, N])
        x_shift = sb("x_shift", [ROWS0, CHUNKS0, N])
        x_rep = sb("x_rep", [P, LOADS + TWICE, CPL, N])
        whole = sb("whole", [P, WHOLE_SLOTS, 2, N])
        head = sb("head", [P, SPLIT_SLOTS, 2, N], F32R)
        rest = sb("rest", [P, SPLIT_SLOTS, 2, N], F32R)
        w0a, w0b = (whole[:, slot].rearrange("p a n -> p (a n)")[:, 0:CHUNKS0 * UNITS]
                    .rearrange("p (c s) -> p c s", s=UNITS) for slot in range(2))
        direct01 = sb("direct01", [P, TOGETHER, N])
        direct2 = sb("direct2", [P, TOGETHER, N])
        part = sb("part", [P, P])
        w_loaded = {layer: place.rearrange("p c n -> p (c n)")[:, 0:CHUNKS * UNITS]
                    .rearrange("p (c s) -> p c s", s=UNITS)
                    for layer, place in ((1, x_rep[:, LOADS:].rearrange("p g c n -> p (g c) n")),
                                         (2, whole[:, 2:5].rearrange("p w a n -> p (w a) n")))}
        flat = x_rep[:].rearrange("p g c n -> p (g c n)")
        at = [0]

        def in_x_rep(rows, size):
            at[0] += size
            return flat[0:rows, at[0] - size:at[0]]

        wt1 = in_x_rep(P, 2 * T1).rearrange("p (c m) -> p c m", c=2)
        wt1c = in_x_rep(CTX, T1)
        wt2 = in_x_rep(P, M1 * T2).rearrange("p (c m) -> p c m", c=M1)
        assert at[0] <= TWICE * CPL * N
        h1 = in_x_rep(P, M1 * B).rearrange("p (m n) -> p m n", m=M1)
        h2 = in_x_rep(P, M2 * B).rearrange("p (m n) -> p m n", m=M2)
        y_row = in_x_rep(1, B)
        sum01 = sb("sum01", [P, B])
        sum2 = sb("sum2", [P, B])

        z = [bank("z_even"), bank("z_odd")]
        x0_bank = [bank("x0_even"), bank("x0_odd")]
        x1_bank = bank("x1_bank")
        x2_bank = bank("x2_bank")
        whole_psum = ctx.enter_context(nc.psum_tensor("whole_psum", [P, 2, N], F32))
        mlp = [whole_psum[:, 0, :], whole_psum[:, 1, :], x0_bank[0][:], x0_bank[1][:]]

        s_w0_ext = sem("w0_extended")
        s_w0_load = sem("w0_loaded")
        s_w0_zero = sem("w0_zeroed")
        s_w0 = sem("w0_ready")
        s_w12_zero = sem("w12_zeroed")
        s_w = sem("weights_loaded")
        s_ident0 = sem("ident_zeroed")
        s_ident = sem("ident_ready")
        s_ids = sem("ids_loaded")
        s_idx = sem("idx_ready")
        s_gather = sem("gather_landed")
        s_emb = sem("emb_ready")
        s_x0 = sem("x0_transposed")
        s_xt = sem("xt_ready")
        s_stored = sem("x_rows_stored")
        s_shift = sem("x_shift_loaded")
        s_rep = [sem(f"x_rep_loaded_{g}") for g in range(LOADS + TWICE)]
        s_prod = sem("products_made")
        s_head = sem("heads_made")
        s_rest_p = sem("rests_made_by_pool")
        s_rest_v = sem("rests_made_by_vector")
        s_used = sem("products_used")
        s_split_h = sem("weight_heads_made")
        s_split = sem("weights_split")
        s_wt = sem("top_weights_loaded")
        s_x1 = sem("x1_ready")
        s_x2 = sem("x2_ready")
        s_d01 = sem("direct01_ready")
        s_d2 = sem("direct2_ready")
        s_part01 = sem("part01_ready")
        s_part2 = sem("part2_ready")
        s_sum01 = sem("sum01_ready")
        s_sum2 = sem("sum2_ready")
        s_ctx_t = sem("ctx_transposed")
        s_ctx = sem("ctx_ready")
        s_mm = sem("mlp_bank_full")
        s_act = sem("mlp_bank_read")
        s_out = sem("y_stored")

        def before(t, layer, j, kinds="UPV"):
            def among(which, upto=None):
                return sum(kind in kinds for kind in KINDS[which][:upto])

            here = among(layer, j)
            if t.turn is None and t.first < 0:
                return here
            last = t.turn is None and t.first == TILES - 1
            for which in ORDER[:ORDER.index(layer)]:
                if not (which == 0 and last):
                    here += among(which)
            return t.count(sum(among(which) for which in ORDER), among(0) + here)

        def number(t, layer, j, kinds):
            return before(Tile(t.first), layer, j, kinds)

        def rep_place(t, g):
            return g + LOADS if g < TWICE and t.first % 2 else g

        def wait_rep(eng, t, g):
            eng.wait_ge(s_rep[rep_place(t, g)], t.visits(2, 32, 32) if g < TWICE else t.count(32, 32))

        run_order = [(step, layer, j) for step in range(-1, TILES) for layer in ORDER
                     if (step >= 0 or layer == 0) and (step < TILES - 1 or layer != 0)
                     for j in range(len(KINDS[layer]))]

        def earlier(t, layer, j, kinds, back):
            now = run_order.index((t.first, layer, j))
            found = [x for x in run_order[:now] if KINDS[x[1]][x[2]] in kinds]
            if len(found) < back:
                return None
            step, layer, j = found[-back]
            return Tile(step, t.turn), layer, j

        def kind_of(product):
            return KINDS[product[1]][product[2]]

        def wait_used(eng, product):
            eng.wait_ge(s_used, before(*product) + 1)

        def wait_rest(eng, product):
            kind = kind_of(product)
            eng.wait_ge(s_rest_p if kind == "P" else s_rest_v, before(*product, kind) + 1)

        def split_slot(product):
            return number(*product, "PV") % SPLIT_SLOTS

        def whole_slot(product):
            return whole[:, number(*product, "UP") % WHOLE_SLOTS]

        def stage(t, layer):
            if t.turn is None and t.first < 0:
                return 0
            last = t.turn is None and t.first == TILES - 1
            return t.count(3, {1: 1, 0: 2, 2: 3}[layer] - (1 if last and layer == 2 else 0))

        def z_of(t, layer):
            return z[stage(Tile(t.first), layer) % 2]

        def steps(eng, body, turns=TURNS):
            for t in range(-AHEAD, LOOP0):
                body(Tile(t))
            with eng.Fori(0, turns) as turn:
                for k in range(TPB):
                    body(Tile(LOOP0 + k, turn))
            for t in range(LOOP0 + turns * TPB, TILES):
                body(Tile(t))

        def has_layers12(t):
            return t.turn is not None or t.first >= 0

        def has_layer0(t):
            return t.turn is not None or -1 <= t.first < TILES - 1

        def has_transposes(t):
            return t.turn is not None or t.first < TILES - AHEAD

        mlp_jobs = [(layer, half, m) for layer, chunks in ((1, M1), (2, M2), (3, 1))
                    for half in range(B // N) for m in range(chunks)]

        block = ctx.enter_context(nc.Block())

        @block.sync
        def _(sp):
            sp.dma_start(idx_all[:], ids.rearrange("(b p) f -> p b f", p=P)).then_inc(s_ids, 16)
            sp.dma_start(w0_k[:, 0:FIELDS, :], w0).then_inc(s_w0_ext, 16)
            sp.dma_start(w0_k[:, FIELDS:, :], w0[:, 0:XROWS - FIELDS, :]).then_inc(s_w0_ext, 16)
            sp.dma_start(w0_h[0:FIELDS, :, :], w0).then_inc(s_w0_ext, 16)
            sp.dma_start(w0_h[FIELDS:, :, :], w0[0:XROWS - FIELDS, :, :]).then_inc(s_w0_ext, 16)
            sp.wait_ge(s_w0_ext, 64)
            sp.wait_ge(s_w0_zero, 2)
            kf = w0_k.rearrange("h k s -> (h k) s")
            hf = w0_h.rearrange("h k s -> (h k) s")
            for r in range(SPC):
                n = CHUNKS0 - (SPC * (CHUNKS0 - 1) + r >= SHIFTS)
                rows = slice(FIELDS * r, FIELDS * (r + 1))
                sp.dma_start(w0a[rows, 0:n, :], bass.AP(
                    tensor=kf.tensor, offset=r * UNITS,
                    ap=[[(XROWS + 1) * UNITS, FIELDS], [SPC * UNITS, n], [1, UNITS]])).then_inc(s_w0_load, 16)
                c0 = 1 if r == 0 else 0
                sp.dma_start(w0b[rows, c0:n, :], bass.AP(
                    tensor=hf.tensor, offset=(SPC * c0 + r) * FIELDS * UNITS,
                    ap=[[(FIELDS + 1) * UNITS, FIELDS], [SPC * FIELDS * UNITS, n - c0],
                        [1, UNITS]])).then_inc(s_w0_load, 16)
            whole_rows = (CHUNKS - 1) * P
            sp.wait_ge(s_w12_zero, 2)
            for layer, w in ((1, w1), (2, w2)):
                rows = w.rearrange("h k s -> (h k) s")
                sp.dma_start(w_loaded[layer][:, 0:CHUNKS - 1, :],
                             rows[0:whole_rows].rearrange("(c p) s -> p c s", p=P)).then_inc(s_w, 16)
                sp.dma_start(w_loaded[layer][0:HALF, CHUNKS - 1, :], rows[whole_rows:]).then_inc(s_w, 16)
            for n, b in enumerate((b0, b1, b2)):
                sp.dma_start(bias[:, n:n + 1], b.rearrange("(s a) -> s a", a=1)).then_inc(s_w, 16)
            sp.dma_start(bias_t1[:], b_top1.rearrange("(m p) -> p m", p=P),
                         allow_slow_non_contiguous=True).then_inc(s_w, 16)
            sp.dma_start(bias_t2[:], b_top2.rearrange("(m p) -> p m", p=P),
                         allow_slow_non_contiguous=True).then_inc(s_w, 16)
            sp.dma_start(wt3[:], W_top3.rearrange("(c p) a -> p (c a)", p=P),
                         allow_slow_non_contiguous=True).then_inc(s_w, 16)
            sp.dma_start(ctx_rows[:], dense_ctx.rearrange("(b p) c -> p b c", p=P)).then_inc(s_w, 16)

            def source(row, first, pattern):
                return bass.AP(tensor=row.tensor, offset=row.offset + first * N, ap=pattern)

            def load_rep(t, groups):
                nxt = t.plus(1)
                row = x_rows[nxt.count(1)] if nxt.turn is None else x_rows[bass.ds(nxt.count(1), 1)]
                for g in groups:
                    user = t.plus(-1) if g < TWICE else t
                    if user.turn is not None or user.first >= 0:
                        sp.wait_ge(s_prod, before(user, 2, (g + 1) * (CPL // 2)))
                    elif t.first == 0 and g == 0:
                        sp.wait_ge(s_split, 1)
                    for half in range(2):
                        src = source(row, 2 * CPL * g + half, [[0, HALF], [2 * N, CPL], [1, N]])
                        place = rep_place(nxt, g)
                        sp.dma_start(x_rep[HALF * half:HALF * (half + 1), place], src).then_inc(s_rep[place], 16)

            def body(t):
                if has_layer0(t):
                    load_rep(t, range(TWICE))
                if has_transposes(t):
                    nxt = t.plus(AHEAD)
                    row = x_rows[nxt.count(1)] if nxt.turn is None else x_rows[bass.ds(nxt.count(1), 1)]
                    wait(sp, s_xt, nxt.count(1, 1))
                    now = xt[:, nxt.first % 2, :]
                    sp.dma_start(source(row, 0, [[N, FIELDS], [1, N]]), now).then_inc(s_stored, 16)
                    if has_layer0(t):
                        sp.wait_ge(s_prod, before(t, 0, PAIRS0))
                    sp.dma_start(source(row, FIELDS, [[N, XROWS - FIELDS], [1, N]]),
                                 now[0:XROWS - FIELDS, :]).then_inc(s_stored, 16)
                    wait(sp, s_stored, nxt.count(32, 32))
                    for r in range(SPC):
                        src = source(row, r, [[N, FIELDS], [SPC * N, CHUNKS0], [1, N]])
                        sp.dma_start(x_shift[FIELDS * r:FIELDS * (r + 1), :, :], src).then_inc(s_shift, 16)
                if has_layer0(t):
                    load_rep(t, range(TWICE, LOADS))

            steps(sp, body)
            sp.wait_ge(s_prod, before(Tile(TILES - 2), 2, PAIRS))
            sp.dma_start(wt1, W_top1[0:2 * P].rearrange("(c p) m -> p c m", p=P)).then_inc(s_wt, 16)
            sp.dma_start(wt1c, W_top1[2 * P:]).then_inc(s_wt, 16)
            sp.dma_start(wt2, W_top2.rearrange("(c p) m -> p c m", p=P)).then_inc(s_wt, 16)
            sp.wait_ge(s_w0_load, 16 * 2 * SPC)
            sp.wait_ge(s_out, 16)

        @block.gpsimd
        def _(pool):
            def new_indices(b):
                src = idx_all[:, b, :] if isinstance(b, int) else idx_all[:, bass.ds(b, 1), :]
                nc.gpsimd.tensor_copy(idx[:], src).then_inc(s_idx, 1)

            def gather(f):
                nc.gpsimd.indirect_dma_start(
                    gathered[:, f, :], None, tables[f],
                    bass.IndirectOffsetOnAxis(ap=idx[:, f:f + 1], axis=0)).then_inc(s_gather, 16)

            def rests(t, layer, fields, refill=None):
                split = [j for j, kind in enumerate(KINDS[layer]) if kind == "P"]
                for j in split:
                    product = t, layer, j
                    if j == split[-1] and refill is not None:
                        refill()
                    pool.wait_ge(s_head, before(t, layer, j, "PV") + 1)
                    nc.gpsimd.tensor_tensor(rest[:, split_slot(product)], whole_slot(product),
                                            head[:, split_slot(product)].bitcast(F32),
                                            ALU.subtract).then_inc(s_rest_p, 1)
                    if layer == 2 and fields:
                        gather(fields.pop(0))
                for f in fields:
                    gather(f)

            pool.wait_ge(s_ids, 16)
            new_indices(0)
            pool.wait_ge(s_idx, 1)
            for f in range(FIELDS):
                gather(f)
            pool.wait_ge(s_ident0, 1)
            nc.gpsimd.affine_select(out=ident[:], in_=ident[:], compare_op=ALU.not_equal, fill=1.0, base=0,
                                    pattern=[[-1, P]], channel_multiplier=1).then_inc(s_ident, 1)
            pool.wait_ge(s_emb, 1)
            new_indices(1)
            pool.wait_ge(s_idx, 2)
            early = list(range(FIELDS))
            for f in early[:13]:
                gather(f)
            del early[:13]
            per_tile = -(-FIELDS // TPB)

            def body(t):
                if not has_layers12(t):
                    return
                ahead = t.plus(AHEAD)
                k = ahead.first % TPB
                refill = None
                if t.turn is None and t.first < LOOP0:
                    fields = early[:13]
                    del early[:13]
                elif t.turn is None and ahead.blocks(1, 1) >= BLOCKS:
                    fields = []
                else:
                    fields = list(range(k * per_tile, min((k + 1) * per_tile, FIELDS)))
                    if k == 0:
                        def refill():
                            pool.wait_ge(s_emb, ahead.blocks(1, 1))
                            new_indices(ahead.blocks(1, 1))
                            pool.wait_ge(s_idx, ahead.blocks(1, 2))
                rests(t, 1, fields[:GATHERS_BETWEEN], refill)
                rests(t, 2, fields[GATHERS_BETWEEN:])

            steps(pool, body, TURNS - 1)

        @block.scalar
        def _(act):
            act.wait_ge(s_w, 16 * WEIGHT_LOADS)

            for n, (layer, c) in enumerate(split_chunks):
                mm = nc.scalar.copy(w_head[:, n, :], w_loaded[layer][:, c, :])
            mm.then_inc(s_split_h, 1)

            def relu(out, z_rows, b):
                return nc.scalar.activation(out, z_rows, ACT.Relu, bias=b)

            def heads(t, layer, upto=None, start=0):
                split = [j for j, kind in enumerate(KINDS[layer]) if kind != "U"]
                for j in split[start:upto]:
                    product = t, layer, j
                    act.wait_ge(s_prod, before(t, layer, j) + 1)
                    last = earlier(t, layer, j, "PV", SPLIT_SLOTS)
                    if last is not None:
                        wait_used(act, last)
                    src = whole_slot(product) if kind_of(product) == "P" else whole_psum[:]
                    nc.scalar.copy(head[:, split_slot(product)], src).then_inc(s_head, 1)

            def out_layer2(t):
                act.wait_ge(s_used, before(t, 2, PAIRS))
                if t.first % TOGETHER == 0:
                    wait(act, s_sum2, t.visits(TOGETHER))
                relu(direct2[:, t.first % TOGETHER, :], z_of(t, 2)[:], bias[:, 2:3]).then_inc(s_d2, 1)

            def body(t):
                if has_layers12(t):
                    heads(t, 1, upto=HEADS_IN_1)
                    if t.turn is not None or t.first > 0:
                        out_layer2(t.plus(-1))
                if has_transposes(t):
                    nxt = t.plus(AHEAD)
                    if nxt.first % TPB == 0:
                        act.wait_ge(s_gather, nxt.blocks(16 * FIELDS, 16 * FIELDS))
                        wait(act, s_x0, nxt.count(1))
                        nc.scalar.copy(emb[:], gathered[:].rearrange("p f d -> p (f d)").unsqueeze(1)
                                       .to_broadcast([P, SPC, FIELDS * DIM])).then_inc(s_emb, 1)
                    act.wait_ge(s_x0, nxt.count(1, 1))
                    wait(act, s_stored, nxt.count(32, -32))
                    nc.scalar.copy(xt[:, nxt.first % 2, :],
                                   x0_bank[nxt.first % 2][0:FIELDS, :]).then_inc(s_xt, 1)
                if not has_layers12(t) and has_layer0(t):
                    act.wait_ge(s_ctx_t, 1)
                    for half in range(B // N):
                        nc.scalar.copy(ctx_t[:, half * N:(half + 1) * N], mlp[half][0:CTX, :]).then_inc(s_ctx, 1)
                if has_layers12(t):
                    heads(t, 1, start=HEADS_IN_1)
                    zz = z_of(t, 1)
                    act.wait_ge(s_used, before(t, 1, PAIRS))
                    relu(x2_bank[0:HALF, :], zz[0:HALF, :], bias[0:HALF, 1:2]).then_inc(s_x2, 1)
                    relu(x2_bank[HALF:P, :], zz[0:HALF, :], bias[0:HALF, 1:2]).then_inc(s_x2, 1)
                    if t.first % TOGETHER == 0:
                        wait(act, s_sum01, t.visits(TOGETHER))
                    relu(direct01[HALF:P, t.first % TOGETHER, :], zz[HALF:P, :],
                         bias[HALF:P, 1:2]).then_inc(s_d01, 1)
                    heads(t, 2, upto=HEADS_IN_2)
                if has_layer0(t):
                    nxt = t.plus(1)
                    zz = z_of(t, 0)
                    act.wait_ge(s_used, before(t, 0, PAIRS0))
                    relu(x1_bank[0:HALF, :], zz[0:HALF, :], bias[0:HALF, 0:1]).then_inc(s_x1, 1)
                    relu(x1_bank[HALF:P, :], zz[0:HALF, :], bias[0:HALF, 0:1]).then_inc(s_x1, 1)
                    if nxt.first % TOGETHER == 0:
                        wait(act, s_sum01, nxt.visits(TOGETHER))
                    relu(direct01[0:HALF, nxt.first % TOGETHER, :], zz[HALF:P, :],
                         bias[HALF:P, 0:1]).then_inc(s_d01, 1)
                if has_layers12(t):
                    heads(t, 2, start=HEADS_IN_2)

            steps(act, body)
            out_layer2(Tile(TILES - 1))
            for n, (layer, half, m) in enumerate(mlp_jobs):
                cols = slice(half * N, (half + 1) * N)
                full = mlp[n % len(mlp)]
                act.wait_ge(s_mm, n + 1)
                if layer == 1:
                    relu(h1[:, m, cols], full, bias_t1[:, m:m + 1]).then_inc(s_act, 1)
                elif layer == 2:
                    relu(h2[:, m, cols], full, bias_t2[:, m:m + 1]).then_inc(s_act, 1)
                else:
                    nc.scalar.copy(y_row[:, cols], full[0:1, :]).then_inc(s_act, 1)
            act.wait_ge(s_act, len(mlp_jobs))
            act.dma_start(y.rearrange("b a -> a b"), y_row).then_inc(s_out, 16)
            act.wait_ge(s_out, 16)

        @block.vector
        def _(dve):
            for w in (w0a, w0b):
                nc.vector.memset(w, 0.0).then_inc(s_w0_zero, 1)
            for w in w_loaded.values():
                nc.vector.memset(w[HALF:P, CHUNKS - 1, :], 0.0).then_inc(s_w12_zero, 1)
            nc.vector.memset(ident[:], 0.0).then_inc(s_ident0, 1)
            dve.wait_ge(s_w0_load, 16 * 2 * SPC)
            nc.vector.tensor_tensor(w0s[0:ROWS0], w0a[0:ROWS0], w0b[0:ROWS0], ALU.add).then_inc(s_w0, 1)
            dve.wait_ge(s_w0, 1)
            dve.wait_ge(s_w, 16 * WEIGHT_LOADS)
            for n, (layer, c) in enumerate(whole_chunks):
                nc.vector.tensor_copy(w_whole[:, n, :], w_loaded[layer][:, c, :])
            dve.wait_ge(s_split_h, 1)
            for n, (layer, c) in enumerate(split_chunks):
                last = nc.vector.tensor_tensor(w_rest[:, n, :], w_loaded[layer][:, c, :],
                                               w_head[:, n, :].bitcast(F32), ALU.subtract)
            last.then_inc(s_split, 1)

            def product(t, layer, j, xk, x0, rows):
                now = t, layer, j
                if kind_of(now) == "V":
                    out = whole_psum
                    last = earlier(t, layer, j, "V", 1)
                    if last is not None:
                        wait_rest(dve, last)
                else:
                    out = whole_slot(now)
                    last = earlier(t, layer, j, "UP", WHOLE_SLOTS)
                    if last is not None and kind_of(last) == "U":
                        wait_used(dve, last)
                    elif last is not None:
                        wait_rest(dve, last)
                width = x0.shape[1]
                nc.vector.tensor_tensor(out[0:rows, 0:width, :],
                                        xk[0:rows, :].unsqueeze(1).to_broadcast([rows, width, N]),
                                        x0, ALU.mult).then_inc(s_prod, 1)

            def rest_of(product):
                dve.wait_ge(s_head, before(*product, "PV") + 1)
                nc.vector.tensor_tensor(rest[:, split_slot(product)], whole_psum[:],
                                        head[:, split_slot(product)].bitcast(F32),
                                        ALU.subtract).then_inc(s_rest_v, 1)

            def layer12(t, layer, xk, between):
                later = []
                for j in range(PAIRS):
                    if layer == 1 and (2 * j) % CPL == 0:
                        wait_rep(dve, t, 2 * j // CPL)
                    c = 2 * j % CPL
                    product(t, layer, j, xk, x_rep[:, rep_place(t, 2 * j // CPL), c:c + 2, :], P)
                    if KINDS[layer][j] == "V":
                        later.append(j)
                    if j in between:
                        between[j]()
                    while later and (later[0] <= j - DEFER or j == PAIRS - 1 or
                                     KINDS[layer][j + 1] == "V"):
                        rest_of((t, layer, later.pop(0)))

            def add_dims(out, direct, t, done, partial):
                b = t.blocks()
                cols = out[:, b * P:(b + 1) * P] if t.turn is None else out[:, bass.ds(b * P, P)]
                grouped = direct[:].rearrange("p t (d b) -> p b (t d)", d=DPT)
                if t.first % TPB < TOGETHER:
                    nc.vector.tensor_reduce(cols, grouped, AX_X, ALU.add).then_inc(done, 1)
                else:
                    nc.vector.tensor_reduce(part[:], grouped, AX_X, ALU.add).then_inc(partial, 1)
                    dve.wait_ge(done, t.visits(TOGETHER))
                    dve.wait_ge(partial, t.blocks(1, 1))
                    nc.vector.tensor_tensor(cols, cols, part[:], ALU.add).then_inc(done, 1)

            def add_layer2(t):
                dve.wait_ge(s_d2, t.count(1, 1))
                add_dims(sum2, direct2, t, s_sum2, s_part2)

            def add_layers01(t):
                dve.wait_ge(s_d01, t.count(2, 2))
                add_dims(sum01, direct01, t, s_sum01, s_part01)

            def body(t):
                if has_layers12(t):
                    dve.wait_ge(s_x1, t.count(2, 2))
                    ends = t.first % TOGETHER == 0 and (t.turn is not None or t.first > 0)
                    layer12(t, 1, x1_bank, {ADD_2_AFTER: lambda: add_layer2(t.plus(-1))} if ends else {})
                if has_layer0(t):
                    nxt = t.plus(1)
                    dve.wait_ge(s_xt, nxt.count(1, 1))
                    dve.wait_ge(s_shift, nxt.count(16 * SPC, 16 * SPC))
                    for j in range(PAIRS0):
                        c = slice(2 * j, min(2 * j + 2, CHUNKS0))
                        product(t, 0, j, x0_bank[nxt.first % 2], x_shift[:, c, :], ROWS0)
                if has_layers12(t):
                    dve.wait_ge(s_x2, t.count(2, 2))
                    ends = t.first % TOGETHER == TOGETHER - 1
                    layer12(t, 2, x2_bank, {ADD_01_AFTER: lambda: add_layers01(t)} if ends else {})

            steps(dve, body)
            add_layer2(Tile(TILES - 1))

        @block.tensor
        def _(pe):
            pe.wait_ge(s_ident, 1)
            pe.wait_ge(s_w0, 1)
            pe.wait_ge(s_split, 1)

            def layer12(t, layer, j):
                zz = z_of(t, layer)
                now = t, layer, j
                if kind_of(now) == "U":
                    pe.wait_ge(s_prod, before(*now) + 1)
                    terms = [(w_whole[:, whole_chunks.index((layer, 2 * j + i)), :], whole_slot(now)[:, i, :])
                             for i in range(2)]
                else:
                    wait_rest(pe, now)
                    terms = []
                    for i in range(2):
                        n = split_chunks.index((layer, 2 * j + i))
                        hd, rs = head[:, split_slot(now), i, :], rest[:, split_slot(now), i, :]
                        terms += [(w_rest[:, n, :], hd), (w_head[:, n, :], hd), (w_head[:, n, :], rs)]
                for i, (w, x) in enumerate(terms):
                    mm = nc.tensor.matmul(zz[:], w, x, start=(j == 0 and i == 0),
                                          stop=(j == PAIRS - 1 and i == len(terms) - 1))
                mm.then_inc(s_used, 1)

            def layer0(t, j):
                pe.wait_ge(s_prod, before(t, 0, j) + 1)
                for i in range(2 * j, min(2 * j + 2, CHUNKS0)):
                    mm = nc.tensor.matmul(z_of(t, 0)[:], w0s[0:ROWS0, i, :],
                                          whole_slot((t, 0, j))[0:ROWS0, i - 2 * j, :],
                                          start=(i == 0), stop=(i == CHUNKS0 - 1))
                mm.then_inc(s_used, 1)

            def body(t):
                if has_layers12(t):
                    wait(pe, s_d01, t.count(2, 1))
                    for j in range(TRANSPOSES_AFTER):
                        layer12(t, 1, j)
                if has_transposes(t):
                    nxt = t.plus(AHEAD)
                    if nxt.first % TPB == 0:
                        wait(pe, s_emb, nxt.blocks(1, 1))
                    if has_layers12(t):
                        pe.wait_ge(s_prod, before(t.plus(-1), 0, PAIRS0))
                    out = x0_bank[nxt.first % 2]
                    for i in range(DPT):
                        d = nxt.first % TPB * DPT + i
                        rows = emb[:].rearrange("p r (f d) -> p (r f) d", d=DIM)[:, :, d]
                        mm = nc.tensor.transpose(out[0:ROWS0, i * P:(i + 1) * P], rows, ident[:])
                    mm.then_inc(s_x0, 1)
                    if not has_layers12(t) and has_layer0(t):
                        for b in range(BLOCKS):
                            mm = nc.tensor.transpose(mlp[b * P // N][0:CTX, b * P % N:b * P % N + P],
                                                     ctx_rows[:, b, :], ident[:])
                        mm.then_inc(s_ctx_t, 1)
                if has_layers12(t):
                    for j in range(TRANSPOSES_AFTER, PAIRS):
                        layer12(t, 1, j)
                if has_layer0(t):
                    if has_layers12(t):
                        wait(pe, s_d2, t.count(1))
                    for j in range(PAIRS0):
                        layer0(t, j)
                if has_layers12(t):
                    if has_layer0(t):
                        wait(pe, s_d01, t.count(2, 2))
                    else:
                        wait(pe, s_d2, t.count(1))
                    for j in range(PAIRS):
                        layer12(t, 2, j)

            steps(pe, body)

            pe.wait_ge(s_ctx, 2)
            pe.wait_ge(s_wt, 48)
            for n, (layer, half, m) in enumerate(mlp_jobs):
                cols = slice(half * N, (half + 1) * N)
                units = slice(m * P, (m + 1) * P)
                out = mlp[n % len(mlp)]
                if layer == 1:
                    terms = [(wt1c[:, units], ctx_t[:, cols]), (wt1[:, 0, units], sum01[:, cols]),
                             (wt1[:, 1, units], sum2[:, cols])]
                    if m == 0:
                        pe.wait_ge(s_sum01, TILES // TOGETHER * (half + 1) // (B // N))
                        pe.wait_ge(s_sum2, TILES // TOGETHER * (half + 1) // (B // N))
                elif layer == 2:
                    terms = [(wt2[:, c, units], h1[:, c, cols]) for c in range(M1)]
                else:
                    terms = [(wt3[:, c:c + 1], h2[:, c, cols]) for c in range(M2)]
                    out = out[0:1, :]
                inputs_done = mlp_jobs.index((layer - 1, half, 0)) + (M1, M2)[layer - 2] if layer > 1 else 0
                needed = max(n - len(mlp) + 1, inputs_done)
                if needed > 0:
                    pe.wait_ge(s_act, needed)
                for i, (w, x) in enumerate(terms):
                    mm = nc.tensor.matmul(out, w, x, start=(i == 0), stop=(i == len(terms) - 1))
                mm.then_inc(s_mm, 1)


def kernel(**inputs):
    import numpy as np
    import concourse.bacc as bacc
    from concourse.bass_utils import run_bass_kernel_spmd

    tables = [f"tbl_{f}" for f in range(FIELDS)]
    rest = ["W_top1", "b_top1", "W_top2", "b_top2", "W_top3",
            "L0_rec_w0", "L0_rec_w1", "L0_rec_w2", "L0_rec_b0", "L0_rec_b1", "L0_rec_b2"]
    nc = bacc.Bacc("TRN2", target_bir_lowering=False, num_devices=1)
    arrays, aps = {}, {}
    for name in ["dense_ctx", "ids"] + tables + rest:
        a = np.ascontiguousarray(inputs[name])
        arrays["in_" + name] = a
        aps[name] = nc.dram_tensor("in_" + name, a.shape, mybir.dt.from_np(a.dtype), kind="ExternalInput").ap()
    y = nc.dram_tensor("y", (inputs["ids"].shape[0], 1), F32, kind="ExternalOutput").ap()
    build_kernel(nc, aps["dense_ctx"], aps["ids"], [aps[t] for t in tables], *[aps[n] for n in rest], y)
    result = run_bass_kernel_spmd(nc, [arrays], core_ids=[0])
    return result.results[0]["y"]
```
